# Optimizing a Trainium2 kernel written in Bass

```python
import numpy as np
import jax
import jax.numpy as jnp

def _softmax(x, axis=-1):
    return jax.nn.softmax(x, axis=axis)

def _gelu(x):
    return jax.nn.gelu(x, approximate=True)

def _silu(x):
    return jax.nn.silu(x)

def _sigmoid(x):
    return jax.nn.sigmoid(x)

def _layernorm(x, axis=-1, eps=1e-05):
    m = jnp.mean(x, axis=axis, keepdims=True)
    v = jnp.var(x, axis=axis, keepdims=True)
    return (x - m) / jnp.sqrt(v + eps)

def _scatter_add(tgt, idx, src, axis=0):
    return tgt.at[idx].add(src)

def _segment_sum(src, seg, n):
    return jax.ops.segment_sum(src, seg, n)
kernel_name = 'mk_audio_tower_d2_tok_aud1d768_r4_823f70'

def setup_inputs(seed: int=0):
    np.random.seed(seed)
    _w = jnp.asarray

    def _rec_inputs():
        import jax
        import jax.numpy as jnp
        _rk = jax.random.key(seed)
        x = -6.41493e-05 + 1.00002 * jax.random.normal(jax.random.fold_in(_rk, 1), (16, 40000), jnp.float32)
        return x
    x = _rec_inputs()

    def _L0_tok_setup():
        import jax, jax.numpy as jnp
        import numpy as np
        import math
        SR = 4000
        FRAME_LEN = 100
        FRAME_STEP = 160
        N_FILTERS = 40
        N_MFCC = 13
        EMBED = 192
        BATCH = 64
        AUDIO_LEN = 40000
        N_FFT_BINS = FRAME_LEN // 2 + 1

        def _mel_filterbank():
            low_mel = 2595.0 * math.log10(1.0 + 0.0 / 700.0)
            high_mel = 2595.0 * math.log10(1.0 + SR // 2 / 700.0)
            mel_points = np.linspace(low_mel, high_mel, N_FILTERS + 2)
            hz_points = 700.0 * (10.0 ** (mel_points / 2595.0) - 1.0)
            bin_points = np.floor((FRAME_LEN + 1) * hz_points / SR)
            filt = np.zeros((N_FILTERS, N_FFT_BINS), dtype=np.float32)
            for i in range(1, N_FILTERS + 1):
                l, c, r = (bin_points[i - 1], bin_points[i], bin_points[i + 1])
                for j in range(int(l), int(c)):
                    filt[i - 1, j] = (j - l) / (c - l)
                for j in range(int(c), int(r)):
                    filt[i - 1, j] = (r - j) / (r - c)
            return jnp.asarray(filt)

        def _dct_matrix():
            k = np.arange(N_MFCC)[:, None]
            j = np.arange(N_FILTERS)[None, :]
            m = np.cos(np.pi * k * (2 * j + 1) / (2 * N_FILTERS)) * math.sqrt(2.0 / N_FILTERS)
            return jnp.asarray(m.astype(np.float32))
        key = jax.random.key(seed)
        kx, kw = jax.random.split(key)
        x = jax.random.normal(kx, (BATCH, AUDIO_LEN), dtype=jnp.float32)
        bound = 1.0 / math.sqrt(N_MFCC)
        w_proj = jax.random.uniform(kw, (N_MFCC, EMBED), minval=-bound, maxval=bound, dtype=jnp.float32)
        b_proj = jnp.zeros((EMBED,), dtype=jnp.float32)
        return {'x': x, 'mel_filters': _mel_filterbank(), 'dct': _dct_matrix(), 'w_proj': w_proj, 'b_proj': b_proj}
    _L0_tok_all = _L0_tok_setup()
    _L0_tok_in = {k: v for k, v in _L0_tok_all.items() if k in ('mel_filters', 'dct', 'w_proj', 'b_proj')}
    del _L0_tok_all

    def _L0_attn_setup():
        import jax, jax.numpy as jnp
        import numpy as np
        DIM = 192
        HEADS = 12
        HEAD_DIM = DIM // HEADS
        TOPK = 100
        SCALE = HEAD_DIM ** (-0.5)
        key = jax.random.key(seed)
        k1, k2, k3, k4 = jax.random.split(key, 4)
        B, N = (8, 256)
        x = jax.random.normal(k1, (B, N, DIM), dtype=jnp.float32)
        w_qkv = jax.random.normal(k2, (DIM, 3 * DIM), dtype=jnp.float32) * DIM ** (-0.5)
        w_proj = jax.random.normal(k3, (DIM, DIM), dtype=jnp.float32) * DIM ** (-0.5)
        b_proj = jax.random.normal(k4, (DIM,), dtype=jnp.float32) * 0.01
        return {'x': x, 'w_qkv': w_qkv, 'w_proj': w_proj, 'b_proj': b_proj}
    _L0_attn_all = _L0_attn_setup()
    _L0_attn_in = {k: v for k, v in _L0_attn_all.items() if k in ('w_qkv', 'w_proj', 'b_proj')}
    del _L0_attn_all

    def _L0_ffn_setup():
        import jax, jax.numpy as jnp
        import numpy as np
        ALPHA = 1.702
        LIMIT = 7.0
        TOP_K = 2
        B, S, H, E, I = (2, 256, 192, 8, 192)
        key = jax.random.key(seed)
        ks = jax.random.split(key, 7)
        scale = 0.02
        return {'hidden_states': jax.random.normal(ks[0], (B, S, H), dtype=jnp.float32), 'Wr': jax.random.normal(ks[1], (H, E), dtype=jnp.float32) * scale, 'br': jax.random.normal(ks[2], (E,), dtype=jnp.float32) * scale, 'Wgu': jax.random.normal(ks[3], (E, H, 2 * I), dtype=jnp.float32) * scale, 'bgu': jax.random.normal(ks[4], (E, 2 * I), dtype=jnp.float32) * scale, 'Wd': jax.random.normal(ks[5], (E, I, H), dtype=jnp.float32) * scale, 'bd': jax.random.normal(ks[6], (E, H), dtype=jnp.float32) * scale}
    _L0_ffn_all = _L0_ffn_setup()
    _L0_ffn_in = {k: v for k, v in _L0_ffn_all.items() if k in ('Wr', 'br', 'Wgu', 'bgu', 'Wd', 'bd')}
    del _L0_ffn_all

    def _L1_attn_setup():
        import jax, jax.numpy as jnp
        import numpy as np
        NUM_HEADS = 12
        KERNEL_EPS = 0.001

        def _performer_relu_attention(q, k, v, projection):
            d = q.shape[-1]
            data_normalizer = 1.0 / jnp.sqrt(jnp.sqrt(jnp.asarray(d, q.dtype)))
            qp = jax.nn.relu(jnp.einsum('bhnd,md->bhnm', q * data_normalizer, projection)) + KERNEL_EPS
            kp = jax.nn.relu(jnp.einsum('bhnd,md->bhnm', k * data_normalizer, projection)) + KERNEL_EPS
            k_sum = kp.sum(axis=2)
            d_inv = 1.0 / jnp.einsum('bhnm,bhm->bhn', qp, k_sum)
            context = jnp.einsum('bhnm,bhnd->bhmd', kp, v)
            out = jnp.einsum('bhnm,bhmd->bhnd', qp, context) * d_inv[..., None]
            return out
        key = jax.random.key(seed)
        ks = jax.random.split(key, 6)
        B, N, C = (4, 1024, 192)
        H = NUM_HEADS
        d = C // H
        m = 64
        x = jax.random.normal(ks[0], (B, N, C), dtype=jnp.float32)
        w_qkv = jax.random.normal(ks[1], (3 * C, C), dtype=jnp.float32) * 0.02
        b_qkv = jnp.zeros((3 * C,), dtype=jnp.float32)
        w_proj = jax.random.normal(ks[2], (C, C), dtype=jnp.float32) * 0.02
        b_proj = jnp.zeros((C,), dtype=jnp.float32)
        projection = jax.random.normal(ks[3], (m, d), dtype=jnp.float32)
        return {'x': x, 'w_qkv': w_qkv, 'b_qkv': b_qkv, 'w_proj': w_proj, 'b_proj': b_proj, 'projection': projection}
    _L1_attn_all = _L1_attn_setup()
    _L1_attn_in = {k: v for k, v in _L1_attn_all.items() if k in ('w_qkv', 'b_qkv', 'w_proj', 'b_proj', 'projection')}
    del _L1_attn_all

    def _L1_ffn_setup():
        import jax, jax.numpy as jnp
        import numpy as np
        N_EMBD = 192
        EXPERT_SIZES = [(8, 128), (8, 256)]
        TOP_K = 8
        NORM_TOPK_PROB = True
        EXPERT_WIDTHS = []
        for cnt, w in EXPERT_SIZES:
            EXPERT_WIDTHS += [w] * cnt
        EXPERT_OFFSETS = np.concatenate([[0], np.cumsum(EXPERT_WIDTHS)]).astype(np.int64)
        NUM_EXPERTS = len(EXPERT_WIDTHS)
        TOTAL_WIDTH = int(EXPERT_OFFSETS[-1])
        key = jax.random.key(seed)
        k1, k2, k3, k4 = jax.random.split(key, 4)
        x = jax.random.normal(k1, (1, 512, N_EMBD), dtype=jnp.float32)
        router_w = jax.random.normal(k2, (NUM_EXPERTS, N_EMBD), dtype=jnp.float32) * 0.02
        w1 = jnp.clip(jax.random.normal(k3, (N_EMBD, TOTAL_WIDTH), dtype=jnp.float32) * 0.02, -0.06, 0.06)
        w2 = jnp.clip(jax.random.normal(k4, (TOTAL_WIDTH, N_EMBD), dtype=jnp.float32) * 0.02, -0.06, 0.06)
        return {'x': x, 'router_w': router_w, 'w1': w1, 'w2': w2}
    _L1_ffn_all = _L1_ffn_setup()
    _L1_ffn_in = {k: v for k, v in _L1_ffn_all.items() if k in ('router_w', 'w1', 'w2')}
    del _L1_ffn_all
    return {'x': x, 'L0_tok_mel_filters': _L0_tok_in['mel_filters'], 'L0_tok_dct': _L0_tok_in['dct'], 'L0_tok_w_proj': _L0_tok_in['w_proj'], 'L0_tok_b_proj': _L0_tok_in['b_proj'], 'L0_attn_w_qkv': _L0_attn_in['w_qkv'], 'L0_attn_w_proj': _L0_attn_in['w_proj'], 'L0_attn_b_proj': _L0_attn_in['b_proj'], 'L0_ffn_Wr': _L0_ffn_in['Wr'], 'L0_ffn_br': _L0_ffn_in['br'], 'L0_ffn_Wgu': _L0_ffn_in['Wgu'], 'L0_ffn_bgu': _L0_ffn_in['bgu'], 'L0_ffn_Wd': _L0_ffn_in['Wd'], 'L0_ffn_bd': _L0_ffn_in['bd'], 'L1_attn_w_qkv': _L1_attn_in['w_qkv'], 'L1_attn_b_qkv': _L1_attn_in['b_qkv'], 'L1_attn_w_proj': _L1_attn_in['w_proj'], 'L1_attn_b_proj': _L1_attn_in['b_proj'], 'L1_attn_projection': _L1_attn_in['projection'], 'L1_ffn_router_w': _L1_ffn_in['router_w'], 'L1_ffn_w1': _L1_ffn_in['w1'], 'L1_ffn_w2': _L1_ffn_in['w2']}

def reference(x, L0_tok_mel_filters, L0_tok_dct, L0_tok_w_proj, L0_tok_b_proj, L0_attn_w_qkv, L0_attn_w_proj, L0_attn_b_proj, L0_ffn_Wr, L0_ffn_br, L0_ffn_Wgu, L0_ffn_bgu, L0_ffn_Wd, L0_ffn_bd, L1_attn_w_qkv, L1_attn_b_qkv, L1_attn_w_proj, L1_attn_b_proj, L1_attn_projection, L1_ffn_router_w, L1_ffn_w1, L1_ffn_w2):
    import jax
    import jax.numpy as jnp

    def _L0_tok_ref(x, mel_filters, dct, w_proj, b_proj):
        import jax, jax.numpy as jnp
        import numpy as np
        import math
        SR = 4000
        FRAME_LEN = 100
        FRAME_STEP = 160
        N_FILTERS = 40
        N_MFCC = 13
        EMBED = 192
        BATCH = 64
        AUDIO_LEN = 40000
        N_FFT_BINS = FRAME_LEN // 2 + 1

        def _mel_filterbank():
            low_mel = 2595.0 * math.log10(1.0 + 0.0 / 700.0)
            high_mel = 2595.0 * math.log10(1.0 + SR // 2 / 700.0)
            mel_points = np.linspace(low_mel, high_mel, N_FILTERS + 2)
            hz_points = 700.0 * (10.0 ** (mel_points / 2595.0) - 1.0)
            bin_points = np.floor((FRAME_LEN + 1) * hz_points / SR)
            filt = np.zeros((N_FILTERS, N_FFT_BINS), dtype=np.float32)
            for i in range(1, N_FILTERS + 1):
                l, c, r = (bin_points[i - 1], bin_points[i], bin_points[i + 1])
                for j in range(int(l), int(c)):
                    filt[i - 1, j] = (j - l) / (c - l)
                for j in range(int(c), int(r)):
                    filt[i - 1, j] = (r - j) / (r - c)
            return jnp.asarray(filt)

        def _dct_matrix():
            k = np.arange(N_MFCC)[:, None]
            j = np.arange(N_FILTERS)[None, :]
            m = np.cos(np.pi * k * (2 * j + 1) / (2 * N_FILTERS)) * math.sqrt(2.0 / N_FILTERS)
            return jnp.asarray(m.astype(np.float32))
        B, T = x.shape
        n_frames = 1 + (T - FRAME_LEN) // FRAME_STEP
        idx = jnp.arange(n_frames)[:, None] * FRAME_STEP + jnp.arange(FRAME_LEN)[None, :]
        frames = x[:, idx]
        window = 0.54 - 0.46 * jnp.cos(2.0 * jnp.pi * jnp.arange(FRAME_LEN, dtype=jnp.float32) / (FRAME_LEN - 1))
        windowed = frames * window
        fft = jnp.fft.rfft(windowed, axis=-1)
        power = fft.real ** 2 + fft.imag ** 2
        mel_energies = jnp.einsum('bnf,mf->bnm', power, mel_filters)
        log_energies = jnp.log(mel_energies + 1e-06)
        mfcc = jnp.einsum('bnm,km->bnk', log_energies, dct)
        out = mfcc @ w_proj + b_proj
        return out

    def _L0_attn_ref(x, w_qkv, w_proj, b_proj):
        import jax, jax.numpy as jnp
        import numpy as np
        DIM = 192
        HEADS = 12
        HEAD_DIM = DIM // HEADS
        TOPK = 100
        SCALE = HEAD_DIM ** (-0.5)
        B, N, C = x.shape
        qkv = (x @ w_qkv).reshape(B, N, 3, HEADS, HEAD_DIM)
        qkv = jnp.transpose(qkv, (2, 0, 3, 1, 4))
        q, k, v = (qkv[0], qkv[1], qkv[2])
        attn = jnp.einsum('bhnd,bhmd->bhnm', q, k) * SCALE
        kth = jax.lax.top_k(attn, TOPK)[0][..., -1:]
        attn = jnp.where(attn >= kth, attn, -jnp.inf)
        attn = jax.nn.softmax(attn, axis=-1)
        out = jnp.einsum('bhnm,bhmd->bhnd', attn, v)
        out = jnp.transpose(out, (0, 2, 1, 3)).reshape(B, N, C)
        return out @ w_proj + b_proj

    def _L0_ffn_ref(hidden_states, Wr, br, Wgu, bgu, Wd, bd):
        import jax, jax.numpy as jnp
        import numpy as np
        ALPHA = 1.702
        LIMIT = 7.0
        TOP_K = 2
        B, S, H, E, I = (2, 256, 192, 8, 192)
        logits = jnp.einsum('bsh,he->bse', hidden_states, Wr) + br
        topk_vals, topk_idx = jax.lax.top_k(logits, TOP_K)
        router_scores = jax.nn.softmax(topk_vals, axis=-1)
        gu = jnp.einsum('bsh,ehf->bsef', hidden_states, Wgu) + bgu
        gu = jnp.minimum(gu, LIMIT)
        gate = gu[..., :I]
        up = jnp.maximum(gu[..., I:], -LIMIT)
        glu = gate * jax.nn.sigmoid(gate * ALPHA)
        activated = (up + 1.0) * glu
        down = jnp.einsum('bsei,eih->bseh', activated, Wd) + bd
        sel = jnp.take_along_axis(down, topk_idx[..., None], axis=2)
        output = jnp.sum(sel * router_scores[..., None], axis=2)
        return output

    def _L1_attn_ref(x, w_qkv, b_qkv, w_proj, b_proj, projection):
        import jax, jax.numpy as jnp
        import numpy as np
        NUM_HEADS = 12
        KERNEL_EPS = 0.001

        def _performer_relu_attention(q, k, v, projection):
            d = q.shape[-1]
            data_normalizer = 1.0 / jnp.sqrt(jnp.sqrt(jnp.asarray(d, q.dtype)))
            qp = jax.nn.relu(jnp.einsum('bhnd,md->bhnm', q * data_normalizer, projection)) + KERNEL_EPS
            kp = jax.nn.relu(jnp.einsum('bhnd,md->bhnm', k * data_normalizer, projection)) + KERNEL_EPS
            k_sum = kp.sum(axis=2)
            d_inv = 1.0 / jnp.einsum('bhnm,bhm->bhn', qp, k_sum)
            context = jnp.einsum('bhnm,bhnd->bhmd', kp, v)
            out = jnp.einsum('bhnm,bhmd->bhnd', qp, context) * d_inv[..., None]
            return out
        B, N, C = x.shape
        H = NUM_HEADS
        d = C // H
        qkv = x @ w_qkv.T + b_qkv
        qkv = qkv.reshape(B, N, 3, H, d).transpose(0, 3, 2, 1, 4)
        q, k, v = (qkv[:, :, 0], qkv[:, :, 1], qkv[:, :, 2])
        out = _performer_relu_attention(q, k, v, projection)
        out = out.transpose(0, 2, 1, 3).reshape(B, N, C)
        return out @ w_proj.T + b_proj

    def _L1_ffn_ref(x, router_w, w1, w2):
        import jax, jax.numpy as jnp
        import numpy as np
        N_EMBD = 192
        EXPERT_SIZES = [(8, 128), (8, 256)]
        TOP_K = 8
        NORM_TOPK_PROB = True
        EXPERT_WIDTHS = []
        for cnt, w in EXPERT_SIZES:
            EXPERT_WIDTHS += [w] * cnt
        EXPERT_OFFSETS = np.concatenate([[0], np.cumsum(EXPERT_WIDTHS)]).astype(np.int64)
        NUM_EXPERTS = len(EXPERT_WIDTHS)
        TOTAL_WIDTH = int(EXPERT_OFFSETS[-1])
        B, S, D = x.shape
        xt = x.reshape(-1, D)
        T = xt.shape[0]
        logits = jnp.einsum('td,ed->te', xt, router_w)
        probs = jax.nn.softmax(logits, axis=-1)
        topk_w, topk_idx = jax.lax.top_k(probs, TOP_K)
        if NORM_TOPK_PROB:
            topk_w = topk_w / jnp.sum(topk_w, axis=-1, keepdims=True)
        comb = jnp.zeros((T, NUM_EXPERTS), dtype=xt.dtype)
        comb = comb.at[jnp.arange(T)[:, None], topk_idx].add(topk_w)
        out = jnp.zeros_like(xt)
        for e in range(NUM_EXPERTS):
            off = int(EXPERT_OFFSETS[e])
            wd = EXPERT_WIDTHS[e]
            h = jax.nn.gelu(xt @ w1[:, off:off + wd])
            out = out + comb[:, e:e + 1] * (h @ w2[off:off + wd, :])
        return out.reshape(B, S, D)
    h = _L0_tok_ref(x, L0_tok_mel_filters, L0_tok_dct, L0_tok_w_proj, L0_tok_b_proj)
    h = h + _L0_attn_ref(_layernorm(h, axis=-1), L0_attn_w_qkv, L0_attn_w_proj, L0_attn_b_proj)
    h = h + _L0_ffn_ref(_layernorm(h, axis=-1), L0_ffn_Wr, L0_ffn_br, L0_ffn_Wgu, L0_ffn_bgu, L0_ffn_Wd, L0_ffn_bd)
    h = h + _L1_attn_ref(_layernorm(h, axis=-1), L1_attn_w_qkv, L1_attn_b_qkv, L1_attn_w_proj, L1_attn_b_proj, L1_attn_projection)
    h = h + _L1_ffn_ref(_layernorm(h, axis=-1), L1_ffn_router_w, L1_ffn_w1, L1_ffn_w2)
    return h

_drawn_inputs = setup_inputs


def setup_inputs(seed=0):
    import zlib

    import numpy as np

    out = dict(_drawn_inputs(seed))
    spreads = {'L0_tok_b_proj': (0.0, 0.326), 'L1_attn_b_qkv': (0.0, 0.8), 'L1_attn_b_proj': (0.0, 0.328)}
    factors = {'L0_attn_b_proj': 8.0,
     'L0_ffn_Wr': 8.0,
     'L0_ffn_br': 8.0,
     'L0_ffn_Wgu': 7.474,
     'L0_ffn_bgu': 8.0,
     'L0_ffn_Wd': 7.902,
     'L0_ffn_bd': 21.905,
     'L1_attn_w_qkv': 3.145,
     'L1_attn_w_proj': 3.034,
     'L1_attn_projection': 64.0,
     'L1_ffn_router_w': 8.0,
     'L1_ffn_w1': 8.0,
     'L1_ffn_w2': 8.0}
    for name, (base, spread) in spreads.items():
        noise = np.random.default_rng([zlib.crc32(name.encode()), seed]).standard_normal(out[name].shape)
        drawn = base * np.exp(spread * noise) if base else spread * noise
        out[name] = jnp.asarray(drawn.astype(out[name].dtype))
    for name, factor in factors.items():
        out[name] = (out[name] * factor).astype(out[name].dtype)
    return out
```

```python
from contextlib import ExitStack

import numpy as np

import concourse.bass as bass
from concourse import mybir

F32 = mybir.dt.float32
ALU = mybir.AluOpType
ACT = mybir.ActivationFunctionType
AX = mybir.AxisListType

B = 16
P = 125
N = 2 * P
G = 2 * B
C = 192
HEADS = 12
DH = C // HEADS
VW = DH + 1
FRAME = 100
BINS = FRAME // 2 + 1
MELS = 40
MFCC = 13
TOPK = 100
E0 = 8
T0 = E0 * C // 128
E1 = 16
T1 = 24
M = 64
EPS_LN = 1e-5
EPS_LOG = 1e-6
EPS_RELU = 1e-3
ALPHA = 1.702
LIMIT = 7.0
BIG = 3.0e38
CH = 2 * N
NCH = B * N // CH
ROUNDS = (TOPK + 7) // 8
KT = [(0, 128), (1, C - 128)]


class Chain:

    def __init__(self, eng, sem):
        self.eng, self.sem, self.k = eng, sem, 0

    def start(self):
        self.eng.sem_clear(self.sem)
        self.k = 0

    def mark(self, ins):
        self.k += 1
        ins.then_inc(self.sem, 1)

    def wait(self):
        self.eng.wait_ge(self.sem, self.k)

    def link(self, ins):
        self.mark(ins)
        self.wait()


def ge(eng, sem, value):
    if isinstance(value, int) and value <= 0:
        return
    eng.wait_ge(sem, value)


def batches(eng, body):
    body(0, 0, True, False)
    body(1, 1, False, False)
    with eng.Fori(2, B - 2, 2) as i:
        body(i, 0, False, False)
        body(i + 1, 1, False, False)
    body(B - 2, 0, False, False)
    body(B - 1, 1, False, True)


def build(nc, d, out):
    with ExitStack() as ctx:
        def sb(name, shape):
            return ctx.enter_context(nc.sbuf_tensor(name, shape, F32))

        def sem(name):
            return ctx.enter_context(nc.semaphore(name))

        bank = [ctx.enter_context(nc.psum_tensor(f"bank{i}", [128, 512], F32)) for i in range(8)]

        w = {name: sb("w_" + name, list(ap.shape)) for name, ap in d.items() if name != "frames"}

        h = sb("h", [P, G, C])
        arena = sb("arena", [128, 12 * 1000])
        at = [0]

        def phase():
            at[0] = 0

        def own(shape):
            n = int(np.prod(shape[1:]))
            at[0] += n
            assert at[0] <= arena.shape[1]
            v = arena[0:shape[0], at[0] - n:at[0]]
            names = "abcde"[:len(shape) - 1]
            if len(names) == 1:
                return v
            sizes = {k: x for k, x in zip(names, shape[1:])}
            return v.rearrange(f"p ({' '.join(names)}) -> p {' '.join(names)}", **sizes)
        ones = sb("ones", [1, 128])
        c_log = sb("c_log", [128, 1])
        c_ln = sb("c_ln", [128, 1])

        phase()
        frames = own([FRAME, B * N])
        sq = own([BINS, 2, 2, CH])
        lge = own([MELS, 2, CH])
        mf = own([MFCC, 2, CH])

        st6 = sb("st6", [P, 2, 6])
        mvb = sb("mvb", [P, 2, 2])
        hb = sb("hb", [P, 2, C])
        carrier = sb("carrier", [128, 4])
        mv = [sb(f"mv{i}", [P, G, 2]) for i in range(4)]
        std = sb("std", [P, G, 1])
        rstd = [sb(f"rstd{i}", [P, G, 1]) for i in range(4)]
        xn = sb("xn", [P, 2, 2, C])
        xT = sb("xT", [128, 2, 2, N])

        phase()
        qk = own([128, 2, 3, 2, N])
        vaug = sb("vaug", [P, 2, 2, HEADS, VW])
        s_sb = own([P, 2, 2, N])
        work = own([P, 2, N])
        m8 = sb("m8", [P, 2, 2, 8])
        nmx = sb("nmx", [P, 2, 2, 1])
        e_sb = own([P, 2, 2, N])
        p_sb = own([P, 2, 2, N])
        pT = own([P, 2, 2, N])
        rsum = sb("rsum", [P, 2, HEADS, 1])
        o_sb = sb("o_sb", [P, 2, HEADS, DH])
        oT = sb("oT", [128, 2, N])

        lg = sb("lg", [P, 2, 16])
        rep = sb("rep", [P, 2, 16])
        r8 = sb("r8", [P, 2, 8])
        t8 = sb("t8", [P, 2, 8])
        dl = sb("dl", [P, 2, 16])
        el = sb("el", [P, 2, 16])
        em = sb("em", [P, 2, 16])
        den = sb("den", [P, 2, 1])
        rden = sb("rden", [P, 2, 1])
        comb = sb("comb", [P, 2, 16])
        combT = sb("combT", [16, 2, N])
        phase()
        crows = [own([1, E0 * N])]
        cbcs = [own([128, 2, E0, N])]
        cmid = own([128, 2, E0 // 2, N])
        gate = own([128, 2, N])
        tanh = own([128, 2, N])
        up = own([128, 2, N])
        gc = own([128, 2, N])
        act = own([128, 2, N])
        phase()
        crows.append(own([1, E1 * N]))
        cbcs.append(own([128, 2, E1, N]))
        hid = sb("hid", [128, 2, 2, N])
        gl = sb("gl", [128, 2, 2, N])
        osb = sb("osb", [P, 2, 2, C])
        bd2 = sb("bd2", [E0, C])
        bup1 = sb("bup1", [128, T0])

        phase()
        qT = own([128, 2, 2, 2, N])
        bhalf = sb("bhalf", [128, 4])
        qp = own([128, 2 * 3, N])
        kp = own([P, 2, HEADS * M])
        cbd = sb("cbd", [128, HEADS // 2, 2 * VW])

        loaded = {n: sem("ld_" + n) for n in ("tok", "a", "b", "c", "d")}
        consts_set = sem("consts_set")
        bd2_set, bhalf_set, bup1_set = sem("bd2_set"), sem("bhalf_set"), sem("bup1_set")
        cmid_set = sem("cmid_set")
        dft_ps, sq_set = sem("dft_ps"), sem("sq_set")
        mel_ps, log_set = sem("mel_ps"), sem("log_set")
        dct_ps, mfcc_set = sem("dct_ps"), sem("mfcc_set")
        tok_ps, tok_set = sem("tok_ps"), sem("tok_set")
        stat_step = sem("stat_step")
        stat_set = [sem(f"stat_set{i}") for i in range(4)]
        std_set = [sem(f"std_set{i}") for i in range(4)]
        rstd_set = [sem(f"rstd_set{i}") for i in range(4)]
        xn_set = [sem(f"xn_set{i}") for i in range(4)]
        xt_ps = [sem(f"xt_ps{i}") for i in range(4)]
        xt_set = [sem(f"xt_set{i}") for i in range(4)]
        qk_ps, qk_set = sem("qk_ps"), sem("qk_set")
        v_ps, v_set = sem("v_ps"), sem("v_set")
        s_ps, s_set = sem("s_ps"), sem("s_set")
        top_step = sem("top_step")
        nmx_set, e_set, p_set = sem("nmx_set"), sem("e_set"), sem("p_set")
        pt_ps, pt_set, pv_ps = sem("pt_ps"), sem("pt_set"), sem("pv_ps")
        rsum_set = [sem("rsum_setA"), sem("rsum_setC")]
        o_set = [sem("o_setA"), sem("o_setC")]
        ot_ps = [sem("ot_psA"), sem("ot_psC")]
        ot_set = [sem("ot_setA"), sem("ot_setC")]
        proj_ps = [sem("proj_psA"), sem("proj_psC")]
        h_set = {k: sem("h_set_" + k) for k in "ABCD"}
        lg_ps = [sem("lg_ps0"), sem("lg_ps1")]
        rt_step = sem("rt_step")
        dl_set = [sem("dl_set0"), sem("dl_set1")]
        el_set = [sem("el_set0"), sem("el_set1")]
        comb_set = [sem("comb_set0"), sem("comb_set1")]
        ct_ps = [sem("ct_ps0"), sem("ct_ps1")]
        ct_set = [sem("ct_set0"), sem("ct_set1")]
        row_set = [sem("row_set0"), sem("row_set1")]
        bc_set = [sem("bc_set0"), sem("bc_set1")]
        up_ps = [sem("up_ps0"), sem("up_ps1")]
        gate_set, u_set, tanh_set = sem("gate_set"), sem("u_set"), sem("tanh_set")
        gc_set, act_set = sem("gc_set"), sem("act_set")
        gelu_set = sem("gelu_set")
        hid_set = [sem("hid_set0"), sem("hid_set1")]
        down_ps = [sem("down_ps0"), sem("down_ps1")]
        stored = [sem("stored_even"), sem("stored_odd")]
        cq_ps, cq_set = sem("cq_ps"), sem("cq_set")
        cv_ps, cv_set = sem("cv_ps"), sem("cv_set")
        f_ps, f_set = sem("f_ps"), sem("f_set")
        ctx_ps, ctx_set = sem("ctx_ps"), sem("ctx_set")
        co_ps = sem("co_ps")

        block = ctx.enter_context(nc.Block())

        LOADS = {
            "tok": ["dre", "dim", "melT", "dctT", "wtok", "btok"],
            "a": ["ident", "a_qk", "a_v", "a_p", "a_bp"],
            "b": ["b_r", "b_br", "b_g", "b_u", "b_bg", "b_bu", "b_d", "b_bd"],
            "c": ["c_qk", "c_bqk", "c_v", "c_bv", "c_bd", "c_p", "c_bp"],
            "d": ["d_r", "d_1", "d_2"],
        }
        n_loads = {k: 16 * len(v) for k, v in LOADS.items()}
        n_loads["tok"] += 16

        MO = {0: dict(ph=1, E=E0, load="b"), 1: dict(ph=3, E=E1, load="d")}

        def mids(s):
            return s if s < E0 else s - E0

        @block.sync
        def _(sp):
            sp.dma_start(frames, d["frames"]).then_inc(loaded["tok"], 16)
            for k in ("tok", "a", "b", "c", "d"):
                for name in LOADS[k]:
                    sp.dma_start(w[name][:], d[name]).then_inc(loaded[k], 16)

        @block.gpsimd
        def _(pool):
            pool.memset(ones[:], 1.0)
            pool.memset(c_log[:], EPS_LOG)
            pool.memset(c_ln[:], EPS_LN)
            pool.memset(vaug[:], 1.0)
            pool.memset(cbd[:], 0.0)
            pool.memset(lg[:], -BIG)
            pool.memset(carrier[0:1, 1:4], 0.0)
            pool.memset(t8[:], -BIG).then_inc(consts_set, 1)

            def spread(m, b, p):
                E = MO[m]["E"]
                pool.wait_ge(row_set[m], (b + 1) * 16)
                ge(pool, hid_set[m], (b - 1) * 12)
                pool.tensor_tensor(carrier[0:1, 1:2], carrier[0:1, 2:3], carrier[0:1, 2:3], ALU.add)
                ins = pool.partition_broadcast(cbcs[m][:, p, :, :].rearrange("q e n -> q (e n)"),
                                               crows[m])
                ins.then_inc(bc_set[m], 1)
                if m == 0:
                    pool.wait_ge(bc_set[0], b + 1)
                    pool.tensor_tensor(carrier[0:1, 1:2], carrier[0:1, 2:3], carrier[0:1, 2:3], ALU.add)
                    for lo in (0, 1):
                        ins = pool.tensor_copy(cmid[64 * lo:64 * lo + 64, p, :, :],
                                               cbcs[0][64 * lo:64 * lo + 64, p, lo:E:2, :])
                    ins.then_inc(cmid_set, 1)

            for m in (0, 1):
                def body(b, p, first, last, m=m):
                    if first:
                        spread(m, 0, 0)
                    if not last:
                        spread(m, b + 1, 1 - p)
                batches(pool, body)

        @block.tensor
        def _(pe):
            ident = w["ident"]

            def bias_row(dst, row, start, **kw):
                return pe.matmul(dst, ones[0:1, 0:P], row, start=start, stop=False, **kw)

            def two_k(dst, lhs, rhs, start=True, **kw):
                for t, rows in KT:
                    ins = pe.matmul(dst, lhs(t, rows), rhs(t, rows), start=start and t == 0,
                                    stop=t == 1, **kw)
                return ins

            def transposes(src, dst):
                for t, rows in KT:
                    for half in (0, 1):
                        ins = pe.transpose(dst[0:rows, t * N + half * P:t * N + half * P + P],
                                           src[:, half, 128 * t:128 * t + rows], ident[0:P, 0:P])
                return ins

            def x_transpose(ph, b, p):
                pe.wait_ge(xn_set[ph], b + 1)
                transposes(xn[:, p, :, :], bank[0]).then_inc(xt_ps[ph], 1)

            def token_major(dst, b, p, wt, n, bias=None):
                for half in (0, 1):
                    if bias is not None:
                        bias_row(dst[0:P, half * n:half * n + n], bias, True)
                    ins = two_k(dst[0:P, half * n:half * n + n],
                                lambda t, r: xT[0:r, p, t, half * P:half * P + P],
                                lambda t, r: wt[0:r, t, :], start=bias is None)
                return ins

            pe.wait_ge(loaded["tok"], n_loads["tok"])
            pe.wait_ge(consts_set, 1)
            for c in range(NCH + 3):
                if c < NCH:
                    ge(pe, sq_set, c - 1)
                    for i, name in enumerate(("dre", "dim")):
                        ins = pe.matmul(bank[2 * (c % 2) + i][0:BINS, 0:CH], w[name][:],
                                        frames[:, c * CH:(c + 1) * CH], start=True, stop=True)
                    ins.then_inc(dft_ps, 1)
                if 1 <= c <= NCH:
                    k = c - 1
                    pe.wait_ge(sq_set, k + 1)
                    ge(pe, log_set, k)
                    for i in (0, 1):
                        ins = pe.matmul(bank[4][0:MELS, 0:CH], w["melT"][:], sq[:, k % 2, i, :],
                                        start=i == 0, stop=i == 1)
                    ins.then_inc(mel_ps, 1)
                if 2 <= c <= NCH + 1:
                    k = c - 2
                    pe.wait_ge(log_set, k + 1)
                    ge(pe, mfcc_set, k)
                    pe.matmul(bank[5][0:MFCC, 0:CH], w["dctT"][:], lge[:, k % 2, :],
                              start=True, stop=True).then_inc(dct_ps, 1)
                if c >= 3:
                    k = c - 3
                    pe.wait_ge(mfcc_set, k + 1)
                    ge(pe, tok_set, 2 * k)
                    for g in range(4):
                        dst = bank[6 + g // 2][0:P, (g % 2) * C:(g % 2 + 1) * C]
                        bias_row(dst, w["btok"][:], True)
                        ins = pe.matmul(dst, mf[:, k % 2, g * P:(g + 1) * P], w["wtok"][:],
                                        start=False, stop=True)
                    ins.then_inc(tok_ps, 1)

            pe.wait_ge(loaded["a"], n_loads["a"])

            def a_qk(b, p):
                pe.wait_ge(xt_set[0], b + 1)
                for j in range(3):
                    if j != 1:
                        ge(pe, qk_set, 3 * b + j - (j == 2))
                    for i in (0, 1):
                        ins = two_k(bank[1 - j % 2][:, i * N:(i + 1) * N],
                                    lambda t, r: w["a_qk"][0:r, t, j, i, :],
                                    lambda t, r: xT[0:r, p, t, :])
                    ins.then_inc(qk_ps, 1)

            def a_v(b, p):
                pe.wait_ge(qk_set, 3 * b + 2)
                token_major(bank[0], b, p, w["a_v"], C).then_inc(v_ps, 1)

            def a_scores(b, p, s):
                pe.wait_ge(qk_set, 3 * b + s // 4 + 1)
                ge(pe, s_set, 12 * b + s - 1)
                r = 32 * (s % 4)
                for half in (0, 1):
                    ins = pe.matmul(bank[2 + s % 2][0:P, half * N:(half + 1) * N],
                                    qk[r:r + DH, p, s // 4, 0, half * P:half * P + P],
                                    qk[r:r + DH, p, s // 4, 1, :], start=True, stop=True)
                ins.then_inc(s_ps, 1)

            def a_pt(b, p, s):
                pe.wait_ge(p_set, 12 * b + s + 1)
                ge(pe, pt_set, 12 * b + s)
                for kh in (0, 1):
                    for half in (0, 1):
                        ins = pe.transpose(
                            bank[4][0:P, kh * N + half * P:kh * N + half * P + P],
                            p_sb[:, s % 2, half, kh * P:kh * P + P], ident[0:P, 0:P])
                ins.then_inc(pt_ps, 1)

            def a_pv(b, p, s):
                pe.wait_ge(pt_set, 12 * b + s + 1)
                if s == 0:
                    pe.wait_ge(v_set, b + 1)
                    ge(pe, o_set[0], b)
                for half in (0, 1):
                    at = (half * HEADS + s) * VW
                    for kh in (0, 1):
                        ins = pe.matmul(bank[5][0:P, at:at + VW],
                                        pT[:, s % 2, kh, half * P:half * P + P],
                                        vaug[:, p, kh, s, :], start=kh == 0, stop=kh == 1)
                ins.then_inc(pv_ps, 1)

            def o_transpose(k, b, dst):
                pe.wait_ge(o_set[k], b + 1)
                transposes(o_sb[:].rearrange("p g a d -> p g (a d)"), dst).then_inc(ot_ps[k], 1)

            def project(k, b, dst, wp, bp, hs):
                pe.wait_ge(ot_set[k], b + 1)
                ge(pe, hs, b)
                for half in (0, 1):
                    o = dst[0:P, half * C:(half + 1) * C]
                    bias_row(o, bp, True)
                    ins = two_k(o, lambda t, r: oT[0:r, t, half * P:half * P + P],
                                lambda t, r: wp[0:r, t, :], start=False)
                ins.then_inc(proj_ps[k], 1)

            def a_proj(b):
                project(0, b, bank[7], w["a_p"], w["a_bp"][:], h_set["A"])

            def a_body(b, p, first, last):
                if first:
                    x_transpose(0, 0, 0)
                    a_qk(0, 0)
                    a_v(0, 0)
                for s in range(HEADS):
                    a_scores(b, p, s)
                    if s >= 1:
                        a_pt(b, p, s - 1)
                    elif not first:
                        a_pt(b - 1, 1 - p, HEADS - 1)
                    if s >= 2:
                        a_pv(b, p, s - 2)
                    elif not first:
                        a_pv(b - 1, 1 - p, HEADS - 2 + s)
                    if s == 3 and not first:
                        o_transpose(0, b - 1, bank[6])
                    if s == 4 and not first:
                        a_proj(b - 1)
                    if not last:
                        if s == 7:
                            pe.wait_ge(v_set, b + 1)
                            x_transpose(0, b + 1, 1 - p)
                        if s == 8:
                            a_qk(b + 1, 1 - p)
                        if s == 9:
                            a_v(b + 1, 1 - p)

            batches(pe, a_body)
            a_pt(B - 1, 1, HEADS - 1)
            a_pv(B - 1, 1, HEADS - 2)
            a_pv(B - 1, 1, HEADS - 1)
            o_transpose(0, B - 1, bank[6])
            a_proj(B - 1)

            def route(m, b, p):
                pe.wait_ge(xt_set[MO[m]["ph"]], b + 1)
                E = MO[m]["E"]
                ge(pe, ct_set[m], b)
                token_major(bank[4], b, p, w["b_r" if m == 0 else "d_r"], E,
                            w["b_br"][:] if m == 0 else None).then_inc(lg_ps[m], 1)

            def comb_transpose(m, b, p):
                pe.wait_ge(comb_set[m], b + 1)
                E = MO[m]["E"]
                for half in (0, 1):
                    ins = pe.transpose(bank[4][0:E, 64 + half * P:64 + half * P + P],
                                       comb[:, half, 0:E], ident[0:P, 0:P])
                ins.then_inc(ct_ps[m], 1)

            def m_up(m, b, p, s):
                if m == 0:
                    ge(pe, u_set, 12 * b + s - 2)
                    ge(pe, gate_set, 12 * b + s - 2)
                    tiles = [w["b_g"][:, :, 128 * s:128 * s + 128], w["b_u"][:, :, 128 * s:128 * s + 128]]
                else:
                    ge(pe, gelu_set, 12 * b + s - 2)
                    tiles = [w["d_1"][:, :, 128 * t:128 * t + 128] for t in (2 * s, 2 * s + 1)]
                for i, wt in enumerate(tiles):
                    ins = two_k(bank[1 + s % 3][:, i * N:(i + 1) * N],
                                lambda t, r: wt[0:r, t, :], lambda t, r: xT[0:r, p, t, :])
                ins.then_inc(up_ps[m], 1)

            def m_down(m, b, p, s):
                D = bank[5 + p]
                if s == 0:
                    ge(pe, h_set["BD"[m]], b - 1)
                    if m == 0:
                        pe.wait_ge(ct_set[0], b + 1)
                        for half in (0, 1):
                            pe.matmul(D[0:P, half * C:(half + 1) * C],
                                      combT[0:E0, p, half * P:half * P + P], bd2[:],
                                      start=half == 0, stop=False, skip_group_check=True)
                pe.wait_ge(hid_set[m], 12 * b + s + 1)
                for i in range(1 + m):
                    for half in (0, 1):
                        wd = w["b_d"][:, s, :] if m == 0 else w["d_2"][:, 2 * s + i, :]
                        ins = pe.matmul(D[0:P, half * C:(half + 1) * C],
                                        hid[:, s % 2, i, half * P:half * P + P], wd,
                                        start=(m == 1 and s == 0 and i == 0 and half == 0),
                                        stop=(s == 11 and i == m), skip_group_check=True)
                ins.then_inc(down_ps[m], 1)

            def moe(m):
                ph = MO[m]["ph"]
                pe.wait_ge(loaded[MO[m]["load"]], n_loads[MO[m]["load"]])
                if m == 0:
                    pe.wait_ge(bd2_set, 1)

                def body(b, p, first, last):
                    if first:
                        x_transpose(ph, 0, 0)
                        route(m, 0, 0)
                        comb_transpose(m, 0, 0)
                    for s in range(12):
                        m_up(m, b, p, s)
                        if s >= 2:
                            m_down(m, b, p, s - 2)
                        elif not first:
                            m_down(m, b - 1, 1 - p, 10 + s)
                        if not last:
                            if s == 4:
                                x_transpose(ph, b + 1, 1 - p)
                            if s == 5:
                                route(m, b + 1, 1 - p)
                            if s == 8:
                                comb_transpose(m, b + 1, 1 - p)

                batches(pe, body)
                m_down(m, B - 1, 1, 10)
                m_down(m, B - 1, 1, 11)

            moe(0)

            pe.wait_ge(loaded["c"], n_loads["c"])
            bd = w["c_bd"]

            def c_qk(b, p):
                pe.wait_ge(xt_set[2], b + 1)
                ge(pe, cq_set, 4 * b)
                for i in (0, 1):
                    for tile, (_, cols) in enumerate(KT):
                        at = i * C + 128 * tile
                        ins = two_k(bank[1 + i][0:cols, tile * N:(tile + 1) * N],
                                    lambda t, r: w["c_qk"][0:r, t, at:at + cols],
                                    lambda t, r: xT[0:r, p, t, :])
                ins.then_inc(cq_ps, 1)

            def c_v(b, p):
                token_major(bank[0], b, p, w["c_v"], C, w["c_bv"][:]).then_inc(cv_ps, 1)

            def feat_bank(p, u):
                return bank[3 + (7 * p + u) % 2]

            def c_qp(b, p):
                pe.wait_ge(cq_set, 4 * b + 4)
                for u in range(3):
                    ge(pe, f_set, 7 * b + u - 1)
                    for i in (0, 1):
                        pair = 2 * u + i
                        rows, tile, t = (128, 0, pair) if pair < 4 else (C - 128, 1, pair - 4)
                        ins = pe.matmul(feat_bank(p, u)[:, i * N:(i + 1) * N], bd[0:rows, t, :],
                                        qT[0:rows, p, 0, tile, :], start=True, stop=True)
                    ins.then_inc(f_ps, 1)

            def c_kp(b, p):
                for half in (0, 1):
                    for tile, n in ((0, 4), (1, 2)):
                        u = 3 + 2 * half + tile
                        rows = KT[tile][1]
                        ge(pe, f_set, 7 * b + u - 1)
                        pe.matmul(feat_bank(p, u)[0:P, 0:n * 128],
                                  qT[0:rows, p, 1, tile, half * P:half * P + P],
                                  bd[0:rows, 0:n, :], start=True, stop=True).then_inc(f_ps, 1)

            def c_ctx(b, p):
                pe.wait_ge(f_set, 7 * b + 7)
                pe.wait_ge(cv_set, b + 1)
                ge(pe, ot_set[1], b)
                for t in range(HEADS // 2):
                    for half in (0, 1):
                        ins = pe.matmul(bank[5][:, t * 2 * VW:(t + 1) * 2 * VW],
                                        kp[:, half, 128 * t:128 * t + 128],
                                        vaug[:, p, half, 2 * t:2 * t + 2, :],
                                        start=half == 0, stop=half == 1)
                ins.then_inc(ctx_ps, 1)

            def c_out(b, p):
                pe.wait_ge(ctx_set, b + 1)
                ge(pe, o_set[1], b)
                for half in (0, 1):
                    for t in range(HEADS // 2):
                        at = (half * HEADS + 2 * t) * VW
                        ins = pe.matmul(bank[6][0:P, at:at + 2 * VW],
                                        qp[:, t, half * P:half * P + P], cbd[:, t, :],
                                        start=True, stop=True)
                ins.then_inc(co_ps, 1)

            def c_proj(b):
                project(1, b, bank[7], w["c_p"], w["c_bp"][:], h_set["C"])

            def c_body(b, p, first, last):
                if first:
                    x_transpose(2, 0, 0)
                    c_qk(0, 0)
                    c_v(0, 0)
                c_qp(b, p)
                if not first:
                    c_proj(b - 1)
                c_kp(b, p)
                if not last:
                    pe.wait_ge(cv_set, b + 1)
                    x_transpose(2, b + 1, 1 - p)
                c_ctx(b, p)
                if not last:
                    c_qk(b + 1, 1 - p)
                c_out(b, p)
                if not last:
                    c_v(b + 1, 1 - p)
                o_transpose(1, b, bank[5])

            batches(pe, c_body)
            c_proj(B - 1)

            moe(1)

        @block.scalar
        def _(sc):
            sc.wait_ge(consts_set, 1)
            for c in range(NCH + 1):
                if c < NCH:
                    sc.wait_ge(dft_ps, c + 1)
                    ge(sc, mel_ps, c - 1)
                    for i in (0, 1):
                        ins = sc.activation(sq[:, c % 2, i, :], bank[2 * (c % 2) + i][0:BINS, 0:CH],
                                            ACT.Square)
                    ins.then_inc(sq_set, 1)
                if c >= 1:
                    k = c - 1
                    sc.wait_ge(mel_ps, k + 1)
                    ge(sc, dct_ps, k - 1)
                    sc.activation(lge[:, k % 2, :], bank[4][0:MELS, 0:CH], ACT.Ln,
                                  bias=c_log[0:MELS, :]).then_inc(log_set, 1)

            def norm_std(ph):
                sc.wait_ge(stat_set[ph], B)
                sc.activation(std[:], mv[ph][:, :, 1:2], ACT.Sqrt, bias=c_ln[0:P, :]).then_inc(std_set[ph], 1)

            def x_copy(ph, b, p, users):
                sc.wait_ge(xt_ps[ph], b + 1)
                for s, v in users:
                    ge(sc, s, v)
                sc.copy(xT[:, p, 0, :], bank[0][:, 0:N])
                sc.copy(xT[0:C - 128, p, 1, :], bank[0][0:C - 128, N:2 * N]).then_inc(xt_set[ph], 1)

            def o_copy(k, b, src):
                sc.wait_ge(ot_ps[k], b + 1)
                ge(sc, proj_ps[k], b)
                sc.copy(oT[:, 0, :], src[:, 0:N])
                sc.copy(oT[0:C - 128, 1, :], src[0:C - 128, N:2 * N]).then_inc(ot_set[k], 1)

            norm_std(0)

            def a_qk(b, p):
                for j in range(3):
                    sc.wait_ge(qk_ps, 3 * b + j + 1)
                    ge(sc, s_ps, 12 * (b - 1))
                    sc.copy(qk[:, p, j, :, :].rearrange("q i n -> q (i n)"),
                            bank[1 - j % 2][:, 0:2 * N]).then_inc(qk_set, 1)

            def a_v(b, p):
                sc.wait_ge(v_ps, b + 1)
                ge(sc, pv_ps, 12 * (b - 1))
                for half in (0, 1):
                    ins = sc.copy(vaug[:, p, half, :, 0:DH],
                                  bank[0][0:P, half * C:(half + 1) * C].rearrange("p (a d) -> p a d", a=HEADS))
                ins.then_inc(v_set, 1)

            def a_s(b, s):
                sc.wait_ge(s_ps, 12 * b + s + 1)
                ge(sc, p_set, 12 * b + s - 1)
                sc.copy(s_sb[:, s % 2, :, :].rearrange("p g n -> p (g n)"),
                        bank[2 + s % 2][0:P, 0:2 * N]).then_inc(s_set, 1)

            def a_pt(b, s):
                sc.wait_ge(pt_ps, 12 * b + s + 1)
                ge(sc, pv_ps, 12 * b + s - 1)
                sc.copy(pT[:, s % 2, :, :].rearrange("p g n -> p (g n)"),
                        bank[4][0:P, 0:2 * N]).then_inc(pt_set, 1)

            def a_exp(b, s):
                sc.wait_ge(nmx_set, 12 * b + s + 1)
                for half in (0, 1):
                    ins = sc.activation(e_sb[:, s % 2, half, :], s_sb[:, s % 2, half, :], ACT.Exp,
                                        bias=nmx[:, s % 2, half, :], scale=float(DH) ** -0.5)
                ins.then_inc(e_set, 1)

            def a_body(b, p, first, last):
                if first:
                    x_copy(0, 0, 0, [])
                    a_qk(0, 0)
                    a_v(0, 0)
                for s in range(HEADS):
                    a_s(b, s)
                    if s >= 1:
                        a_pt(b, s - 1)
                    elif not first:
                        a_pt(b - 1, HEADS - 1)
                    a_exp(b, s)
                    if s == 3 and not first:
                        o_copy(0, b - 1, bank[6])
                    if not last:
                        if s == 7:
                            x_copy(0, b + 1, 1 - p, [(v_ps, b)])
                        if s == 8:
                            a_qk(b + 1, 1 - p)
                        if s == 9:
                            a_v(b + 1, 1 - p)

            batches(sc, a_body)
            a_pt(B - 1, HEADS - 1)
            o_copy(0, B - 1, bank[6])

            def ct_copy(m, b, p):
                E = MO[m]["E"]
                sc.wait_ge(ct_ps[m], b + 1)
                ge(sc, row_set[m], 16 * (b - 1))
                if m == 0:
                    ge(sc, down_ps[0], 12 * (b - 1))
                sc.copy(combT[0:E, p, :], bank[4][0:E, 64:64 + N]).then_inc(ct_set[m], 1)
                sc.wait_ge(ct_set[m], b + 1)
                ge(sc, bc_set[m], b)
                sc.dma_start(crows[m], combT[0:E, p, :]).then_inc(row_set[m], 16)

            def store(b, p):
                sc.wait_ge(h_set["D"], b + 1)
                sc.dma_start(out[b], osb[:, p, :, :]).then_inc(stored[p], 16)

            def r_exp(m, b):
                E = MO[m]["E"]
                sc.wait_ge(dl_set[m], b + 1)
                sc.activation(el[:, :, 0:E], dl[:, :, 0:E], ACT.Exp).then_inc(el_set[m], 1)

            def moe(m):
                ph = MO[m]["ph"]
                norm_std(ph)

                def body(b, p, first, last):
                    if first:
                        x_copy(ph, 0, 0, [])
                        r_exp(m, 0)
                        ct_copy(m, 0, 0)
                    for s in range(12):
                        if m == 0:
                            sc.wait_ge(gate_set, 12 * b + s + 1)
                            ge(sc, act_set, 12 * b + s - 1)
                            sc.activation(tanh[:, s % 2, :], gate[:, s % 2, :], ACT.Tanh,
                                          scale=ALPHA / 2).then_inc(tanh_set, 1)
                        else:
                            sc.wait_ge(up_ps[1], 12 * b + s + 1)
                            ge(sc, hid_set[1], 12 * b + s - 1)
                            sc.activation(gl[:, s % 2, :, :].rearrange("p i n -> p (i n)"),
                                          bank[1 + s % 3][:, 0:2 * N],
                                          ACT.Gelu_apprx_tanh).then_inc(gelu_set, 1)
                        if m == 1 and s == 5 and not first:
                            store(b - 1, 1 - p)
                        if not last:
                            if s == 4:
                                x_copy(ph, b + 1, 1 - p, [(up_ps[m], 12 * b)])
                            if s == 6:
                                r_exp(m, b + 1)
                            if s == 8:
                                ct_copy(m, b + 1, 1 - p)

                batches(sc, body)

            moe(0)

            norm_std(2)

            def c_qk(b, p):
                sc.wait_ge(cq_ps, b + 1)
                ge(sc, f_ps, 7 * (b - 1))
                for i in (0, 1):
                    for tile, (_, rows) in enumerate(KT):
                        sc.activation(qT[0:rows, p, i, tile, :],
                                      bank[1 + i][0:rows, tile * N:(tile + 1) * N], ACT.Identity,
                                      bias=bhalf[0:rows, 2 * i + tile:2 * i + tile + 1],
                                      scale=float(DH) ** -0.25).then_inc(cq_set, 1)

            def c_v(b, p):
                sc.wait_ge(cv_ps, b + 1)
                ge(sc, ctx_ps, b - 1)
                for half in (0, 1):
                    ins = sc.copy(vaug[:, p, half, :, 0:DH],
                                  bank[0][0:P, half * C:(half + 1) * C].rearrange("p (a d) -> p a d", a=HEADS))
                ins.then_inc(cv_set, 1)

            def c_body(b, p, first, last):
                if first:
                    x_copy(2, 0, 0, [])
                    sc.wait_ge(bhalf_set, 1)
                    c_qk(0, 0)
                    c_v(0, 0)
                if not last:
                    x_copy(2, b + 1, 1 - p, [(cv_ps, b)])
                    c_qk(b + 1, 1 - p)
                    c_v(b + 1, 1 - p)
                o_copy(1, b, bank[5])

            batches(sc, c_body)
            moe(1)
            store(B - 1, 1)
            for p in (0, 1):
                sc.wait_ge(stored[p], 8 * B)

        @block.vector
        def _(dv):
            dv.wait_ge(loaded["c"], n_loads["c"])
            dv.wait_ge(loaded["b"], n_loads["b"])
            dv.wait_ge(consts_set, 1)
            dv.tensor_scalar(bhalf[:], w["c_bqk"][:], float(DH) ** -0.25, None, ALU.mult).then_inc(bhalf_set, 1)
            dv.tensor_scalar(bup1[:], w["b_bu"][:], 1.0, None, ALU.add).then_inc(bup1_set, 1)
            dv.tensor_scalar(bd2[:], w["b_bd"][:], 2.0, None, ALU.mult).then_inc(bd2_set, 1)

            stats = Chain(dv, stat_step)

            def carry():
                dv.memset(carrier[0:1, 0:1], 0.0)

            def statistics(ph, b):
                for half in (0, 1):
                    stats.mark(dv.bn_stats(st6[:, half, :], hb[:, half, :]))
                stats.wait()
                for half in (0, 1):
                    stats.mark(dv.bn_aggr(mvb[:, half, :], st6[:, half, :]))
                stats.wait()
                dv.tensor_copy(mv[ph][:, bass.ds(2 * b, 2), :], mvb[:]).then_inc(stat_set[ph], 1)

            def norm_rstd(ph):
                dv.wait_ge(std_set[ph], 1)
                dv.reciprocal(rstd[ph][:], std[:]).then_inc(rstd_set[ph], 1)
                dv.wait_ge(rstd_set[ph], 1)

            def normalise(ph, b, p):
                ge(dv, xt_ps[ph], b - 1)
                for half in (0, 1):
                    g = 2 * b + half
                    ins = dv.tensor_scalar(xn[:, p, half, :], h[:, g, :], mv[ph][:, g, 0:1],
                                           rstd[ph][:, g, :], ALU.subtract, ALU.mult)
                ins.then_inc(xn_set[ph], 1)

            def residual(ph, b, acc, ready, value, hs):
                stats.start()
                dv.wait_ge(ready, value)
                hv = h[:, bass.ds(2 * b, 2), :].rearrange("p g c -> p (g c)")
                hn = hb[:].rearrange("p g c -> p (g c)")
                ins = dv.tensor_tensor(hn, hv, acc[0:P, 0:2 * C], ALU.add)
                stats.link(ins)
                dv.tensor_copy(hv, hn).then_inc(hs, 1)
                statistics(ph, b)

            for c in range(NCH + 1):
                if c < NCH:
                    dv.wait_ge(dct_ps, c + 1)
                    ge(dv, tok_ps, c - 1)
                    dv.tensor_copy(mf[:, c % 2, :], bank[5][0:MFCC, 0:CH]).then_inc(mfcc_set, 1)
                if c >= 1:
                    k = c - 1
                    dv.wait_ge(tok_ps, k + 1)
                    for j in (0, 1):
                        stats.start()
                        stats.link(dv.tensor_copy(hb[:].rearrange("p g c -> p (g c)"), bank[6 + j][0:P, 0:2 * C]))
                        dv.tensor_copy(h[:, 4 * k + 2 * j:4 * k + 2 * j + 2, :], hb[:]).then_inc(tok_set, 1)
                        statistics(0, 2 * k + j)

            norm_rstd(0)
            top = Chain(dv, top_step)
            scale = float(DH) ** -0.5

            def top_k(b, s):
                dv.wait_ge(s_set, 12 * b + s + 1)
                ge(dv, p_set, 12 * b + s - 1)
                carry()
                top.start()
                src = [s_sb[:, s % 2, half, :] for half in (0, 1)]
                for r in range(ROUNDS):
                    for half in (0, 1):
                        top.mark(dv.max(m8[:, s % 2, half, :], src[half] if r == 0 else work[:, half, :]))
                    top.wait()
                    if r == 0:
                        ge(dv, e_set, 12 * b + s - 1)
                        dv.tensor_scalar(nmx[:, s % 2, :, :], m8[:, s % 2, :, 0:1], -scale, None,
                                         ALU.mult).then_inc(nmx_set, 1)
                    if r < ROUNDS - 1:
                        for half in (0, 1):
                            top.mark(dv.match_replace(work[:, half, :], m8[:, s % 2, half, :],
                                                      src[half] if r == 0 else work[:, half, :], -BIG))
                        top.wait()

            def mask(b, s):
                dv.wait_ge(e_set, 12 * b + s + 1)
                ge(dv, pt_ps, 12 * b + s - 1)
                kth = (TOPK - 1) % 8
                for half in (0, 1):
                    ins = dv.scalar_tensor_tensor(p_sb[:, s % 2, half, :], s_sb[:, s % 2, half, :],
                                                  m8[:, s % 2, half, kth:kth + 1], e_sb[:, s % 2, half, :],
                                                  ALU.is_ge, ALU.mult)
                ins.then_inc(p_set, 1)

            def divide(k, b, src, ready, value):
                dv.wait_ge(ready, value)
                ge(dv, ot_ps[k], b)
                v = src[0:P, 0:2 * HEADS * VW].rearrange("p (g a w) -> p (g a) w", g=2, a=HEADS)
                dv.reciprocal(rsum[:].rearrange("p g a o -> p (g a) o"), v[:, :, DH:VW]).then_inc(rsum_set[k], 1)
                dv.wait_ge(rsum_set[k], b + 1)
                dv.tensor_tensor(o_sb[:].rearrange("p g a d -> p (g a) d"), v[:, :, 0:DH],
                                 rsum[:].rearrange("p g a o -> p (g a) o").to_broadcast([P, 2 * HEADS, DH]),
                                 ALU.mult).then_inc(o_set[k], 1)

            def a_body(b, p, first, last):
                if first:
                    normalise(0, 0, 0)
                for s in range(HEADS):
                    top_k(b, s)
                    mask(b, s)
                    if s == 1 and not first:
                        divide(0, b - 1, bank[5], pv_ps, 12 * b)
                    if s == 5 and not first:
                        residual(1, b - 1, bank[7], proj_ps[0], b, h_set["A"])
                    if s == 5 and not last:
                        normalise(0, b + 1, 1 - p)

            batches(dv, a_body)
            divide(0, B - 1, bank[5], pv_ps, 12 * B)
            residual(1, B - 1, bank[7], proj_ps[0], B, h_set["A"])

            def router(m, b, p, steps):
                E = MO[m]["E"]
                steps.start()
                dv.wait_ge(lg_ps[m], b + 1)
                steps.link(dv.tensor_copy(lg[:, :, 0:E],
                                          bank[4][0:P, 0:2 * E].rearrange("p (g e) -> p g e", g=2)))
                for half in (0, 1):
                    steps.mark(dv.max(r8[:, half, :], lg[:, half, 0:E]))
                steps.wait()
                if m == 0:
                    steps.link(dv.tensor_copy(t8[:, :, 0:2], r8[:, :, 0:2]))
                best = t8 if m == 0 else r8
                dv.tensor_tensor(dl[:, :, 0:E], lg[:, :, 0:E], r8[:, :, 0:1].to_broadcast([P, 2, E]),
                                 ALU.subtract).then_inc(dl_set[m], 1)
                for half in (0, 1):
                    steps.mark(dv.match_replace(rep[:, half, 0:16], best[:, half, :], lg[:, half, 0:16], BIG))
                steps.wait()
                dv.wait_ge(el_set[m], b + 1)
                steps.link(dv.scalar_tensor_tensor(em[:, :, 0:E], rep[:, :, 0:E], BIG / 2, el[:, :, 0:E],
                                                   ALU.is_gt, ALU.mult))
                steps.link(dv.tensor_reduce(den[:], em[:, :, 0:E], AX.X, ALU.add))
                steps.link(dv.reciprocal(rden[:], den[:]))
                ge(dv, ct_ps[m], b)
                if m == 0:
                    steps.link(dv.tensor_scalar(rden[:], rden[:], 0.5, None, ALU.mult))
                dv.tensor_tensor(comb[:, :, 0:E], em[:, :, 0:E],
                                 rden[:].to_broadcast([P, 2, E]), ALU.mult).then_inc(comb_set[m], 1)

            def m0_first(b, p, s):
                U = bank[1 + s % 3]
                dv.wait_ge(up_ps[0], 12 * b + s + 1)
                if s == 0:
                    dv.wait_ge(bup1_set, 1)
                ge(dv, gc_set, 12 * b + s - 1)
                dv.tensor_scalar(gate[:, s % 2, :], U[:, 0:N], w["b_bg"][:, s:s + 1], LIMIT,
                                 ALU.add, ALU.min).then_inc(gate_set, 1)
                ge(dv, hid_set[0], 12 * b + s - 1)
                dv.tensor_scalar(up[:, s % 2, :], U[:, N:2 * N], bup1[:, s:s + 1], LIMIT + 1.0,
                                 ALU.add, ALU.min).then_inc(u_set, 1)
                dv.wait_ge(gate_set, 12 * b + s + 1)
                if s == 0:
                    dv.wait_ge(cmid_set, b + 1)
                c = cbcs[0][:, p, s, :] if s < E0 else cmid[:, p, s - E0, :]
                dv.tensor_tensor(gc[:, s % 2, :], gate[:, s % 2, :], c, ALU.mult).then_inc(gc_set, 1)

            def m0_second(b, p, s):
                dv.wait_ge(tanh_set, 12 * b + s + 1)
                dv.wait_ge(gc_set, 12 * b + s + 1)
                dv.scalar_tensor_tensor(act[:, s % 2, :], tanh[:, s % 2, :], 1.0, gc[:, s % 2, :],
                                        ALU.add, ALU.mult).then_inc(act_set, 1)
                dv.wait_ge(act_set, 12 * b + s + 1)
                dv.wait_ge(u_set, 12 * b + s + 1)
                ge(dv, down_ps[0], 12 * b + s - 1)
                dv.scalar_tensor_tensor(hid[:, s % 2, 0, :], up[:, s % 2, :], 1.0 - LIMIT,
                                        act[:, s % 2, :], ALU.max, ALU.mult).then_inc(hid_set[0], 1)

            def m1_hidden(b, p, s):
                dv.wait_ge(gelu_set, 12 * b + s + 1)
                ge(dv, down_ps[1], 12 * b + s - 1)
                if s == 0:
                    dv.wait_ge(bc_set[1], b + 1)
                if s < 4:
                    c = cbcs[1][:, p, 2 * s:2 * s + 2, :]
                else:
                    c = cbcs[1][:, p, 4 + s:5 + s, :].to_broadcast([128, 2, N])
                dv.tensor_tensor(hid[:, s % 2, :, :], gl[:, s % 2, :, :], c, ALU.mult).then_inc(hid_set[1], 1)

            def finish(m, b, p):
                D = bank[5 + p]
                if m == 0:
                    residual(2, b, D, down_ps[0], 12 * b + 12, h_set["B"])
                else:
                    dv.wait_ge(down_ps[1], 12 * b + 12)
                    ge(dv, stored[p], 8 * (b - p))
                    dv.tensor_tensor(osb[:, p, :, :].rearrange("p g c -> p (g c)"),
                                     h[:, bass.ds(2 * b, 2), :].rearrange("p g c -> p (g c)"),
                                     D[0:P, 0:2 * C], ALU.add).then_inc(h_set["D"], 1)

            def moe(m):
                ph = MO[m]["ph"]
                norm_rstd(ph)
                steps = Chain(dv, rt_step)

                def body(b, p, first, last):
                    if first:
                        normalise(ph, 0, 0)
                        router(m, 0, 0, steps)
                    for s in range(12):
                        if m == 0:
                            m0_first(b, p, s)
                            if s >= 1:
                                m0_second(b, p, s - 1)
                            elif not first:
                                m0_second(b - 1, 1 - p, 11)
                        else:
                            m1_hidden(b, p, s)
                        if s == 3 and not first:
                            finish(m, b - 1, 1 - p)
                        if not last:
                            if s == 3:
                                normalise(ph, b + 1, 1 - p)
                            if s == 6:
                                router(m, b + 1, 1 - p, steps)

                batches(dv, body)
                if m == 0:
                    m0_second(B - 1, 1, 11)
                finish(m, B - 1, 1)

            moe(0)

            norm_rstd(2)

            def feature(dst, src):
                return dv.tensor_scalar(dst, src, 0.0, EPS_RELU, ALU.max, ALU.add)

            def feat_bank(p, u):
                return bank[3 + (7 * p + u) % 2]

            def c_features(b, p):
                for u in range(3):
                    dv.wait_ge(f_ps, 7 * b + u + 1)
                    if u == 0:
                        ge(dv, co_ps, b)
                    feature(qp[:, 2 * u:2 * u + 2, :].rearrange("q i n -> q (i n)"),
                            feat_bank(p, u)[:, 0:2 * N]).then_inc(f_set, 1)

            def c_kfeatures(b, p):
                for half in (0, 1):
                    for tile, at, n in ((0, 0, 512), (1, 512, 256)):
                        u = 3 + 2 * half + tile
                        dv.wait_ge(f_ps, 7 * b + u + 1)
                        feature(kp[:, half, at:at + n], feat_bank(p, u)[0:P, 0:n]).then_inc(f_set, 1)

            def c_context(b, p):
                dv.wait_ge(ctx_ps, b + 1)
                v = bank[5][:, 0:HEADS * VW].rearrange("q (t i w) -> q t i w", t=HEADS // 2, i=2)
                for i in (0, 1):
                    ins = dv.tensor_copy(cbd[64 * i:64 * i + 64, :, i * VW:(i + 1) * VW],
                                         v[64 * i:64 * i + 64, :, i, :])
                ins.then_inc(ctx_set, 1)

            def c_body(b, p, first, last):
                if first:
                    normalise(2, 0, 0)
                c_features(b, p)
                if not last:
                    normalise(2, b + 1, 1 - p)
                c_kfeatures(b, p)
                if not first:
                    residual(3, b - 1, bank[7], proj_ps[1], b, h_set["C"])
                c_context(b, p)
                divide(1, b, bank[6], co_ps, b + 1)

            batches(dv, c_body)
            residual(3, B - 1, bank[7], proj_ps[1], B, h_set["C"])

            moe(1)


def _pack(a):
    z = np.zeros((256, a.shape[1]), a.dtype)
    z[:a.shape[0]] = a
    return z.reshape(2, 128, -1).transpose(1, 0, 2)


def _dft():
    n = np.arange(FRAME)
    window = 0.54 - 0.46 * np.cos(2.0 * np.pi * n / (FRAME - 1))
    angle = 2.0 * np.pi * np.outer(n, np.arange(BINS)) / FRAME
    return [(f(angle) * window[:, None]).astype(np.float32) for f in (np.cos, np.sin)]


def _moe_order():
    e = np.arange(E0)[:, None] * C
    return np.concatenate([(e + np.arange(128)).ravel(), (e + np.arange(128, C)).ravel()])


def kernel(x, L0_tok_mel_filters, L0_tok_dct, L0_tok_w_proj, L0_tok_b_proj, L0_attn_w_qkv,
           L0_attn_w_proj, L0_attn_b_proj, L0_ffn_Wr, L0_ffn_br, L0_ffn_Wgu, L0_ffn_bgu, L0_ffn_Wd,
           L0_ffn_bd, L1_attn_w_qkv, L1_attn_b_qkv, L1_attn_w_proj, L1_attn_b_proj,
           L1_attn_projection, L1_ffn_router_w, L1_ffn_w1, L1_ffn_w2):
    from concourse import bacc
    from concourse.bass_utils import run_bass_kernel_spmd

    a = {}
    x = np.asarray(x)
    a["frames"] = x.reshape(G, P, 160)[:, :, :FRAME].transpose(2, 0, 1).reshape(FRAME, B * N)
    a["dre"], a["dim"] = _dft()
    a["melT"] = np.asarray(L0_tok_mel_filters).T
    a["dctT"] = np.asarray(L0_tok_dct).T
    a["wtok"] = np.asarray(L0_tok_w_proj)
    a["btok"] = np.asarray(L0_tok_b_proj)[None]
    a["ident"] = np.eye(128, dtype=np.float32)

    wqkv = np.asarray(L0_attn_w_qkv)
    z = np.zeros((C, 3, 2, 4, 32), np.float32)
    z[..., :DH] = wqkv[:, :2 * C].reshape(C, 2, 3, 4, DH).transpose(0, 2, 1, 3, 4)
    a["a_qk"] = _pack(z.reshape(C, -1)).reshape(128, 2, 3, 2, 128)
    a["a_v"] = _pack(wqkv[:, 2 * C:])
    a["a_p"] = _pack(np.asarray(L0_attn_w_proj))
    a["a_bp"] = np.asarray(L0_attn_b_proj)[None]

    order = _moe_order()
    wgu = np.asarray(L0_ffn_Wgu).transpose(1, 0, 2)
    bgu = np.asarray(L0_ffn_bgu)
    a["b_r"] = _pack(np.asarray(L0_ffn_Wr))
    a["b_br"] = np.asarray(L0_ffn_br)[None]
    a["b_g"] = _pack(wgu[:, :, :C].reshape(C, E0 * C)[:, order])
    a["b_u"] = _pack(wgu[:, :, C:].reshape(C, E0 * C)[:, order])
    a["b_bg"] = bgu[:, :C].ravel()[order].reshape(T0, 128).T
    a["b_bu"] = bgu[:, C:].ravel()[order].reshape(T0, 128).T
    a["b_d"] = np.asarray(L0_ffn_Wd).reshape(E0 * C, C)[order].reshape(T0, 128, C).transpose(1, 0, 2)
    a["b_bd"] = np.asarray(L0_ffn_bd)

    cw = np.asarray(L1_attn_w_qkv)
    cb = np.asarray(L1_attn_b_qkv)
    a["c_qk"] = _pack(cw[:2 * C].T)
    z = np.zeros((2, 256), np.float32)
    z[:, :C] = cb[:2 * C].reshape(2, C)
    a["c_bqk"] = z.reshape(4, 128).T
    a["c_v"] = _pack(cw[2 * C:].T)
    a["c_bv"] = cb[2 * C:][None]
    z = np.zeros((4, 2, DH, 4, 2, M), np.float32)
    for t in range(4):
        for i in range(2):
            z[t, i, :, t, i, :] = np.asarray(L1_attn_projection).T
    a["c_bd"] = z.reshape(128, 4, 128)
    a["c_p"] = _pack(np.asarray(L1_attn_w_proj).T)
    a["c_bp"] = np.asarray(L1_attn_b_proj)[None]

    a["d_r"] = _pack(np.asarray(L1_ffn_router_w).T)
    a["d_1"] = _pack(np.asarray(L1_ffn_w1))
    a["d_2"] = np.asarray(L1_ffn_w2).reshape(T1, 128, C).transpose(1, 0, 2)

    nc = bacc.Bacc("TRN2", target_bir_lowering=False, num_devices=1)
    arrays, aps = {}, {}
    for name, v in a.items():
        arrays["in_" + name] = np.ascontiguousarray(v)
        aps[name] = nc.dram_tensor("in_" + name, v.shape, F32, kind="ExternalInput").ap()
    y = nc.dram_tensor("out_h", (B, P, 2, C), F32, kind="ExternalOutput").ap()
    build(nc, aps, y)
    r = run_bass_kernel_spmd(nc, [arrays], core_ids=[0])
    return r.results[0]["out_h"].transpose(0, 2, 1, 3).reshape(B, N, C)
```
